# Optimizing a Trainium2 kernel written in Bass

```python
import numpy as np
import jax
import jax.numpy as jnp

def _softmax(x, axis=-1):
    return jax.nn.softmax(x, axis=axis)

def _gelu(x):
    return jax.nn.gelu(x, approximate=True)

def _silu(x):
    return jax.nn.silu(x)

def _sigmoid(x):
    return jax.nn.sigmoid(x)

def _layernorm(x, axis=-1, eps=1e-05):
    m = jnp.mean(x, axis=axis, keepdims=True)
    v = jnp.var(x, axis=axis, keepdims=True)
    return (x - m) / jnp.sqrt(v + eps)

def _scatter_add(tgt, idx, src, axis=0):
    return tgt.at[idx].add(src)

def _segment_sum(src, seg, n):
    return jax.ops.segment_sum(src, seg, n)
kernel_name = 'mk_cond_resid_d2_seqx_r2_403b7f'

def setup_inputs(seed: int=0):
    np.random.seed(seed)
    _w = jnp.asarray

    def _rec_inputs():
        import jax
        import jax.numpy as jnp
        _rk = jax.random.key(seed)
        x = -7.109e-05 + 0.9999 * jax.random.normal(jax.random.fold_in(_rk, 1), (64, 128, 1024), jnp.float32)
        _lenS = 128 - jax.random.randint(jax.random.fold_in(_rk, 7), (64,), 0, max(1, 128 // 4) + 1, jnp.int32)
        _lenS2 = 128 - jax.random.randint(jax.random.fold_in(_rk, 8), (64,), 0, max(1, 128 // 4) + 1, jnp.int32)
        itok_B_1_198 = jax.random.randint(jax.random.fold_in(_rk, 11), (64,), 1, 199, jnp.int32)
        itok_B_0_6 = jax.random.randint(jax.random.fold_in(_rk, 12), (64,), 0, 7, jnp.int32)
        return (x, itok_B_1_198, itok_B_0_6)
    x, itok_B_1_198, itok_B_0_6 = _rec_inputs()

    def _L0_cond_setup():
        import jax, jax.numpy as jnp
        import numpy as np
        B, C, T = (128, 128, 1024)
        S, D = (200, 128)
        key = jax.random.key(seed)
        k1, k2, k3 = jax.random.split(key, 3)
        x = jax.random.normal(k1, (B, C, T), dtype=jnp.float32)
        conditions = jax.random.randint(k2, (B,), 0, S, dtype=jnp.int64)
        weights = jax.random.normal(k3, (S, C, D), dtype=jnp.float32) / jnp.sqrt(jnp.float32(C))
        return {'x': x, 'conditions': conditions, 'weights': weights}
    _L0_cond_all = _L0_cond_setup()
    _L0_cond_in = {k: v for k, v in _L0_cond_all.items() if k in ('weights',)}
    del _L0_cond_all

    def _L1_cond_setup():
        import jax, jax.numpy as jnp
        import numpy as np
        B, T, D_IN, D_OUT = (16, 1024, 1024, 1024)
        N_ADAPTERS, RANK = (8, 16)
        key = jax.random.key(seed)
        k_x, k_w, k_a, k_b, k_s, k_idx = jax.random.split(key, 6)
        x = jax.random.normal(k_x, (B, T, D_IN), dtype=jnp.float32)
        W = jax.random.normal(k_w, (D_OUT, D_IN), dtype=jnp.float32) * (1.0 / np.sqrt(D_IN))
        A = jax.random.normal(k_a, (N_ADAPTERS, RANK, D_IN), dtype=jnp.float32) * 0.02
        Bm = jax.random.normal(k_b, (N_ADAPTERS, D_OUT, RANK), dtype=jnp.float32) * 0.02
        scalings = jnp.ones((N_ADAPTERS,), dtype=jnp.float32)
        adapter_idx = jax.random.randint(k_idx, (B,), 0, N_ADAPTERS, dtype=jnp.int32)
        return {'x': x, 'W': W, 'A': A, 'Bm': Bm, 'scalings': scalings, 'adapter_idx': adapter_idx}
    _L1_cond_all = _L1_cond_setup()
    _L1_cond_in = {k: v for k, v in _L1_cond_all.items() if k in ('W', 'A', 'Bm', 'scalings')}
    del _L1_cond_all
    return {'x': x, 'itok_B_1_198': itok_B_1_198, 'itok_B_0_6': itok_B_0_6, 'L0_cond_weights': _L0_cond_in['weights'], 'L1_cond_W': _L1_cond_in['W'], 'L1_cond_A': _L1_cond_in['A'], 'L1_cond_Bm': _L1_cond_in['Bm'], 'L1_cond_scalings': _L1_cond_in['scalings']}

def reference(x, itok_B_1_198, itok_B_0_6, L0_cond_weights, L1_cond_W, L1_cond_A, L1_cond_Bm, L1_cond_scalings):
    import jax
    import jax.numpy as jnp

    def _L0_cond_ref(x, conditions, weights):
        import jax, jax.numpy as jnp
        import numpy as np
        B, C, T = (128, 128, 1024)
        S, D = (200, 128)
        w = weights[conditions]
        return jnp.einsum('bct,bcd->bdt', x, w)

    def _L1_cond_ref(x, W, A, Bm, scalings, adapter_idx):
        import jax, jax.numpy as jnp
        import numpy as np
        B, T, D_IN, D_OUT = (16, 1024, 1024, 1024)
        N_ADAPTERS, RANK = (8, 16)
        H = jnp.einsum('btd,od->bto', x, W)
        A_b = A[adapter_idx]
        B_b = Bm[adapter_idx]
        s_b = scalings[adapter_idx]
        xa = jnp.einsum('btd,brd->btr', x, A_b)
        delta = jnp.einsum('btr,bor->bto', xa, B_b)
        delta = jax.lax.stop_gradient(delta * s_b[:, None, None])
        return H + delta
    x = x + _L0_cond_ref(x, itok_B_1_198, L0_cond_weights)
    x = x + _L1_cond_ref(x, L1_cond_W, L1_cond_A, L1_cond_Bm, L1_cond_scalings, itok_B_0_6)
    return x

_drawn_inputs = setup_inputs


def setup_inputs(seed=0):
    import zlib

    import numpy as np

    out = dict(_drawn_inputs(seed))
    spreads = {'L1_cond_scalings': (1.0, 0.2)}
    factors = {}
    for name, (base, spread) in spreads.items():
        noise = np.random.default_rng([zlib.crc32(name.encode()), seed]).standard_normal(out[name].shape)
        drawn = base * np.exp(spread * noise) if base else spread * noise
        out[name] = jnp.asarray(drawn.astype(out[name].dtype))
    for name, factor in factors.items():
        out[name] = (out[name] * factor).astype(out[name].dtype)
    return out
```

```python
import concourse.bass as bass
from concourse import mybir
from contextlib import ExitStack

P = 128


def cond_resid_kernel(nc, xT, cond_idx, adapter_idx, cond_w, wT, lora_a, lora_b, scalings, out):
    f32 = mybir.dt.float32
    f32r = mybir.dt.float32r
    i32 = mybir.dt.int32
    ALU = mybir.AluOpType
    ACT = mybir.ActivationFunctionType

    NB, _, KC, C = xT.shape
    T = KC * P
    NCOND = cond_w.shape[0]
    NAD, R = lora_a.shape[1], lora_a.shape[3]
    ROW = T + R
    WIDE = T + 2 * R
    FIRST = (ROW + 5) // 6 * 2
    CUTS = [0, FIRST, FIRST + (ROW - FIRST) // 2, ROW]
    NZ = len(CUTS) - 1
    HALF = T // 2
    BANK = 512

    def pieces(par):
        shift = R if par == 0 else 0
        found = []
        for n in range(NZ):
            lo, hi = max(CUTS[n] - shift, 0), min(CUTS[n + 1] - shift, T)
            found.append((lo + shift - CUTS[n], lo, hi))
        return found

    with ExitStack() as ctx:
        def sb(name, shape, dt):
            return ctx.enter_context(nc.sbuf_tensor(name, shape, dt))

        def sem(name):
            return ctx.enter_context(nc.semaphore(name))

        w_raw = sb("w_raw", [P, KC, T], f32)
        w_hi = sb("w_hi", [P, KC, WIDE], f32r)
        w_lo = sb("w_lo", [P, KC, WIDE], f32r)
        a_tab = sb("a_tab", [P, NAD, KC, R], f32)
        a_now = [sb(f"a_now{j}", [P, KC, R], f32) for j in range(2)]
        s_tab = sb("s_tab", [P, NAD], f32)
        cond_sb = sb("cond_sb", [1, NB], i32)
        adapter_sb = sb("adapter_sb", [1, NB], i32)
        ident = sb("ident", [P, P], f32)
        x_raw = [sb(f"x_raw{j}", [P, KC, C], f32) for j in range(2)]
        x_hi = [sb(f"x_hi{j}", [P, KC, C], f32r) for j in range(2)]
        x_lo = [sb(f"x_lo{j}", [P, KC, C], f32r) for j in range(2)]
        c_raw = [sb(f"c_raw{j}", [P, P], f32) for j in range(2)]
        c_hi = [sb(f"c_hi{j}", [P, P], f32r) for j in range(2)]
        c_lo = [sb(f"c_lo{j}", [P, P], f32r) for j in range(2)]
        b_raw = [sb(f"b_raw{j}", [3 * R, T], f32) for j in range(2)]
        b_stack = [sb(f"b_stack{j}", [P, T], f32r) for j in range(2)]
        xa_cols = sb("xa_cols", [P, P], f32)
        xa_stack = sb("xa_stack", [P, P], f32r)
        z_hi = [sb(f"z_hi{j}", [P, T], f32r) for j in range(2)]
        z_lo = [sb(f"z_lo{j}", [P, T], f32r) for j in range(2)]
        o_sb = [sb(f"o_sb{j}", [P, T], f32) for j in range(2)]

        z_ps = [[ctx.enter_context(nc.psum_tensor(f"z_ps{j}_{n}", [P, BANK], f32)) for n in range(NZ)]
                for j in range(2)]
        o_ps = [ctx.enter_context(nc.psum_tensor(f"o_ps{n}", [P, BANK], f32)) for n in range(2)]
        xaT_ps = o_ps[0]

        idx_landed = sem("idx_landed")
        atab_landed = sem("atab_landed")
        w_landed = [sem(f"w_landed{k}") for k in range(KC)]
        x_landed = [sem(f"x_landed{j}") for j in range(2)]
        c_landed = [sem(f"c_landed{j}") for j in range(2)]
        b_landed = [sem(f"b_landed{j}") for j in range(2)]
        ident_zero = sem("ident_zero")
        ident_ready = sem("ident_ready")
        zeros_ready = sem("zeros_ready")
        atab_scaled = sem("atab_scaled")
        w_summed = sem("w_summed")
        w_hi_ready = sem("w_hi_ready")
        w_lo_ready = sem("w_lo_ready")
        x_hi_ready = sem("x_hi_ready")
        x_lo_ready = sem("x_lo_ready")
        a_picked = sem("a_picked")
        a_hi_ready = sem("a_hi_ready")
        a_ready = sem("a_ready")
        main_done = sem("main_done")
        xa_hi_ready = sem("xa_hi_ready")
        xa_ready = sem("xa_ready")
        xaT_done = sem("xaT_done")
        xaT_ready = sem("xaT_ready")
        b_hi_ready = sem("b_hi_ready")
        b_ready = sem("b_ready")
        z_done = sem("z_done")
        z_hi_ready = sem("z_hi_ready")
        z_lo_ready = sem("z_lo_ready")
        c_summed = sem("c_summed")
        c_hi_ready = sem("c_hi_ready")
        c_lo_ready = sem("c_lo_ready")
        o_done = sem("o_done")
        o_left = sem("o_left")
        o_right = sem("o_right")
        stored = [sem(f"stored{j}") for j in range(2)]

        block = ctx.enter_context(nc.Block())

        def run_steps(eng, step):
            step(0, 0)
            step(0, 1)
            with eng.Fori(1, NB // 2 - 1) as i:
                step(i, 0)
                step(i, 1)
            step(NB // 2 - 1, 0)
            step(NB // 2 - 1, 1)
            step(NB // 2, 0)

        def exists(i, j, d):
            return not isinstance(i, int) or 0 <= 2 * i + j + d < NB

        def done(i, j, d, per=1):
            return (i * 2 + (j + d + 1)) * per

        def landed(i, j, d, per=1):
            return (i + ((j + d) // 2 + 1)) * (16 * per)

        @block.sync
        def _(sp):
            def load_x(i, j, d):
                slot = (j + d) % 2
                b = i * 2 + (j + d)
                if exists(i, j, d - 2):
                    sp.wait_ge(x_lo_ready, done(i, j, d - 2))
                sp.dma_start(x_raw[slot][:, :, :], xT[bass.ds(b, 1), :, :, :].rearrange("b p k c -> (b p) k c"))\
                  .then_inc(x_landed[slot], 16)

            def load_rest(i, j, d):
                slot = (j + d) % 2
                b = i * 2 + (j + d)
                cond = sp.value_load(cond_sb[0:1, bass.ds(b, 1)], min_val=0, max_val=NCOND - 1)
                if exists(i, j, d - 2):
                    sp.wait_ge(c_lo_ready, done(i, j, d - 2))
                sp.dma_start(c_raw[slot][:, :], cond_w[bass.ds(cond, 1), :, :].rearrange("s c d -> (s c) d"))\
                  .then_inc(c_landed[slot], 16)
                adapter = sp.value_load(adapter_sb[0:1, bass.ds(b, 1)], min_val=0, max_val=NAD - 1)
                if exists(i, j, d - 2):
                    sp.wait_ge(b_ready, done(i, j, d - 2))
                for g in range(3):
                    sp.dma_start(b_raw[slot][g * R:(g + 1) * R, :],
                                 lora_b[bass.ds(adapter, 1), :, :].rearrange("a r o -> (a r) o"))\
                      .then_inc(b_landed[slot], 16)

            def step(i, j):
                if exists(i, j, 2):
                    load_x(i, j, 2)
                    load_rest(i, j, 2)
                if exists(i, j, -1):
                    slot = (j - 1) % 2
                    b = i * 2 + (j - 1)
                    sp.wait_ge(o_left, done(i, j, -1))
                    sp.wait_ge(o_right, done(i, j, -1))
                    sp.dma_start(out[bass.ds(b, 1), :, :].rearrange("b d o -> (b d) o"), o_sb[slot][:, :])\
                      .then_inc(stored[slot], 16)

            load_x(0, 0, 0)
            sp.dma_start(cond_sb[:, :], cond_idx).then_inc(idx_landed, 16)
            sp.dma_start(adapter_sb[:, :], adapter_idx).then_inc(idx_landed, 16)
            load_x(0, 0, 1)
            sp.wait_ge(idx_landed, 32)
            load_rest(0, 0, 0)
            load_rest(0, 0, 1)
            run_steps(sp, step)
            for slot in range(2):
                sp.wait_ge(stored[slot], 16 * NB // 2)

        @block.gpsimd
        def _(pool):
            def place_a(i, j, d):
                col = (j + d) % 2 * (T + R)
                b = i * 2 + (j + d)
                adapter = pool.value_load(adapter_sb[0:1, bass.ds(b, 1)], min_val=0, max_val=NAD - 1)
                nc.gpsimd.tensor_copy(a_now[(j + d) % 2][:, :, :],
                                      a_tab[:, bass.ds(adapter, 1), :, :].rearrange("p a k r -> p (a k) r"))\
                    .then_inc(a_picked, 1)
                pool.wait_ge(a_hi_ready, done(i, j, d))
                nc.gpsimd.tensor_tensor(w_lo[:, :, col:col + R], a_now[(j + d) % 2][:, :, :],
                                        w_hi[:, :, col:col + R], ALU.subtract).then_inc(a_ready, 1)

            def step(i, j):
                if exists(i, j, 1):
                    place_a(i, j, 1)

            nc.gpsimd.memset(ident[:, :], 0.0).then_inc(ident_zero, 1)
            pool.wait_ge(ident_zero, 1)
            nc.gpsimd.affine_select(out=ident[:, :], in_=ident[:, :], compare_op=ALU.not_equal, fill=1.0,
                                    base=0, pattern=[[-1, P]], channel_multiplier=1).then_inc(ident_ready, 1)
            nc.gpsimd.memset(xa_cols[:, :], 0.0).then_inc(zeros_ready, 1)
            for slot in range(2):
                nc.gpsimd.memset(b_stack[slot][:, :].bitcast(f32), 0.0).then_inc(zeros_ready, 1)
            pool.wait_ge(idx_landed, 32)
            pool.wait_ge(atab_landed, 32)
            nc.gpsimd.tensor_tensor(
                a_tab[:, :, :, :].rearrange("p a k r -> p a (k r)"),
                a_tab[:, :, :, :].rearrange("p a k r -> p a (k r)"),
                s_tab[:, :].rearrange("p (a o) -> p a o", o=1).to_broadcast([P, NAD, KC * R]),
                ALU.mult).then_inc(atab_scaled, 1)
            pool.wait_ge(atab_scaled, 1)
            place_a(0, 0, 0)
            run_steps(pool, step)

        @block.scalar
        def _(act):
            def split_x(i, j, d):
                slot = (j + d) % 2
                act.wait_ge(x_landed[slot], landed(i, j, d))
                if exists(i, j, d - 2):
                    act.wait_ge(main_done, done(i, j, d - 2))
                nc.scalar.activation(x_hi[slot][:, :, :], x_raw[slot][:, :, :], ACT.Copy).then_inc(x_hi_ready, 1)

            def split_a(i, j, d):
                col = (j + d) % 2 * (T + R)
                act.wait_ge(a_picked, done(i, j, d))
                if exists(i, j, d - 2):
                    act.wait_ge(main_done, done(i, j, d - 2))
                nc.scalar.activation(w_hi[:, :, col:col + R], a_now[(j + d) % 2][:, :, :], ACT.Copy)\
                    .then_inc(a_hi_ready, 1)

            def step(i, j):
                if exists(i, j, 1):
                    split_x(i, j, 1)
                    split_a(i, j, 1)
                if exists(i, j, 0):
                    slot = j % 2
                    act.wait_ge(b_landed[slot], landed(i, j, 0, 3))
                    if exists(i, j, -2):
                        act.wait_ge(z_done, done(i, j, -2, NZ))
                    else:
                        act.wait_ge(zeros_ready, 3)
                    nc.scalar.activation(b_stack[slot][0:3 * R, :], b_raw[slot][:, :], ACT.Copy)\
                        .then_inc(b_hi_ready, 1)
                    act.wait_ge(c_summed, done(i, j, 0))
                    if exists(i, j, -2):
                        act.wait_ge(o_done, done(i, j, -2, 2))
                    nc.scalar.activation(c_hi[slot][:, :], c_raw[slot][:, :], ACT.Copy).then_inc(c_hi_ready, 1)
                if exists(i, j, -1):
                    slot = (j - 1) % 2
                    act.wait_ge(xaT_done, done(i, j, -1))
                    nc.scalar.activation(xa_stack[:, :], xaT_ps[:, 0:P], ACT.Copy).then_inc(xaT_ready, 1)
                    for n, (at, lo, hi) in enumerate(pieces(slot)):
                        act.wait_ge(z_done, done(i, j, -2, NZ) + (n + 1))
                        nc.scalar.activation(z_hi[slot][:, lo:hi], z_ps[slot][n][:, at:at + hi - lo], ACT.Copy)\
                            .then_inc(z_hi_ready, 1)
                    act.wait_ge(o_done, done(i, j, -2, 2) + 1)
                    if exists(i, j, -3):
                        act.wait_ge(stored[slot], landed(i, j, -3))
                    nc.scalar.activation(o_sb[slot][:, 0:HALF], o_ps[0][:, :], ACT.Copy).then_inc(o_left, 1)

            for k in range(KC):
                act.dma_start(w_raw[:, k, :], wT[:, k, :]).then_inc(w_landed[k], 16)
            act.dma_start(a_tab[:, :, :, :], lora_a).then_inc(atab_landed, 16)
            act.dma_start(s_tab[:, :], scalings.to_broadcast([P, NAD])).then_inc(atab_landed, 16)
            split_x(0, 0, 0)
            split_a(0, 0, 0)
            for k in range(KC):
                act.wait_ge(w_summed, k + 1)
                nc.scalar.activation(w_hi[:, k, R:R + T], w_raw[:, k, :], ACT.Copy).then_inc(w_hi_ready, 1)
            run_steps(act, step)

        @block.vector
        def _(dve):
            def split_x(i, j, d):
                slot = (j + d) % 2
                dve.wait_ge(x_hi_ready, done(i, j, d))
                nc.vector.tensor_tensor(x_lo[slot][:, :, :], x_raw[slot][:, :, :], x_hi[slot][:, :, :],
                                        ALU.subtract).then_inc(x_lo_ready, 1)

            def step(i, j):
                if exists(i, j, -1):
                    slot = (j - 1) % 2
                    n, at = (0, 0) if slot == 0 else (NZ - 1, ROW - R - CUTS[NZ - 1])
                    xa = z_ps[slot][n][:, at:at + R]
                    dve.wait_ge(main_done, done(i, j, -1))
                    if exists(i, j, -2):
                        dve.wait_ge(xaT_done, done(i, j, -2))
                    else:
                        dve.wait_ge(zeros_ready, 3)
                    nc.vector.tensor_copy(xa_cols[:, 0:R].bitcast(f32r), xa)
                    nc.vector.tensor_copy(xa_cols[:, 2 * R:3 * R].bitcast(f32r), xa).then_inc(xa_hi_ready, 1)
                    dve.wait_ge(xa_hi_ready, done(i, j, -1))
                    nc.vector.tensor_tensor(xa_cols[:, R:2 * R].bitcast(f32r), xa, xa_cols[:, 0:R],
                                            ALU.subtract).then_inc(xa_ready, 1)
                if exists(i, j, 0):
                    slot = j % 2
                    dve.wait_ge(c_landed[slot], landed(i, j, 0))
                    nc.vector.tensor_tensor(c_raw[slot][:, :], c_raw[slot][:, :], ident[:, :], ALU.add)\
                        .then_inc(c_summed, 1)
                if exists(i, j, 1):
                    split_x(i, j, 1)
                if exists(i, j, 0):
                    dve.wait_ge(b_hi_ready, done(i, j, 0))
                    nc.vector.tensor_tensor(b_stack[slot][2 * R:3 * R, :], b_raw[slot][2 * R:3 * R, :],
                                            b_stack[slot][2 * R:3 * R, :], ALU.subtract).then_inc(b_ready, 1)
                    dve.wait_ge(c_hi_ready, done(i, j, 0))
                    nc.vector.tensor_tensor(c_lo[slot][:, :], c_raw[slot][:, :], c_hi[slot][:, :], ALU.subtract)\
                        .then_inc(c_lo_ready, 1)
                if exists(i, j, -1):
                    slot = (j - 1) % 2
                    for n, (at, lo, hi) in enumerate(pieces(slot)):
                        dve.wait_ge(z_hi_ready, done(i, j, -2, NZ) + (n + 1))
                        nc.vector.tensor_tensor(z_lo[slot][:, lo:hi], z_ps[slot][n][:, at:at + hi - lo],
                                                z_hi[slot][:, lo:hi], ALU.subtract).then_inc(z_lo_ready, 1)
                    dve.wait_ge(o_done, done(i, j, -1, 2))
                    if exists(i, j, -3):
                        dve.wait_ge(stored[slot], landed(i, j, -3))
                    nc.vector.tensor_copy(o_sb[slot][:, HALF:T], o_ps[1][:, :]).then_inc(o_right, 1)

            dve.wait_ge(ident_ready, 1)
            split_x(0, 0, 0)
            for k in range(KC):
                dve.wait_ge(w_landed[k], 16)
                nc.vector.tensor_tensor(w_raw[:, k, k * P:(k + 1) * P], w_raw[:, k, k * P:(k + 1) * P],
                                        ident[:, :], ALU.add).then_inc(w_summed, 1)
                if k >= 1:
                    dve.wait_ge(w_hi_ready, k)
                    nc.vector.tensor_tensor(w_lo[:, k - 1, R:R + T], w_raw[:, k - 1, :],
                                            w_hi[:, k - 1, R:R + T], ALU.subtract).then_inc(w_lo_ready, 1)
            dve.wait_ge(w_hi_ready, KC)
            nc.vector.tensor_tensor(w_lo[:, KC - 1, R:R + T], w_raw[:, KC - 1, :],
                                    w_hi[:, KC - 1, R:R + T], ALU.subtract).then_inc(w_lo_ready, 1)
            run_steps(dve, step)

        @block.tensor
        def _(pe):
            def main_chunk(i, j, k):
                slot = j % 2
                first = 0 if slot == 0 else R
                for left, right in ((x_hi, w_hi), (x_hi, w_lo), (x_lo, w_hi)):
                    for n in range(NZ):
                        start, stop = k == 0 and left is x_hi and right is w_hi, k == KC - 1 and left is x_lo
                        last = nc.tensor.matmul(z_ps[slot][n][:, 0:CUTS[n + 1] - CUTS[n]], left[slot][:, k, :],
                                                right[:, k, first + CUTS[n]:first + CUTS[n + 1]],
                                                start=start, stop=stop)
                return last

            def transpose_xa(i, j):
                pe.wait_ge(xa_ready, done(i, j, -1))
                if exists(i, j, -2):
                    pe.wait_ge(o_left, done(i, j, -2))
                nc.tensor.transpose(xaT_ps[:, 0:P], xa_cols[:, :], ident[:, :]).then_inc(xaT_done, 1)

            def add_lora(i, j):
                slot = (j - 1) % 2
                pe.wait_ge(xaT_ready, done(i, j, -1))
                pe.wait_ge(b_ready, done(i, j, -1))
                for n, (at, lo, hi) in enumerate(pieces(slot)):
                    nc.tensor.matmul(z_ps[slot][n][:, at:at + hi - lo], xa_stack[:, :], b_stack[slot][:, lo:hi],
                                     start=False, stop=True, skip_group_check=True).then_inc(z_done, 1)

            def cond_product(i, j):
                slot = (j - 1) % 2
                pe.wait_ge(c_lo_ready, done(i, j, -1))
                if exists(i, j, -2):
                    pe.wait_ge(o_right, done(i, j, -2))
                for n in range(2):
                    cols = slice(n * HALF, (n + 1) * HALF)
                    need = [m for m, (_, lo, _) in enumerate(pieces(slot)) if lo < (n + 1) * HALF]
                    pe.wait_ge(z_lo_ready, done(i, j, -2, NZ) + len(need))
                    nc.tensor.matmul(o_ps[n][:, :], c_hi[slot][:, :], z_hi[slot][:, cols], start=True, stop=False)
                    nc.tensor.matmul(o_ps[n][:, :], c_hi[slot][:, :], z_lo[slot][:, cols], start=False, stop=False)
                    nc.tensor.matmul(o_ps[n][:, :], c_lo[slot][:, :], z_hi[slot][:, cols], start=False, stop=True)\
                        .then_inc(o_done, 1)

            def step(i, j):
                before = exists(i, j, -1)
                if exists(i, j, 0):
                    pe.wait_ge(x_lo_ready, done(i, j, 0))
                    pe.wait_ge(a_ready, done(i, j, 0))
                    if exists(i, j, -2):
                        pe.wait_ge(z_lo_ready, done(i, j, -2, NZ))
                    for k in range(KC):
                        if not before:
                            pe.wait_ge(w_lo_ready, k + 1)
                        last = main_chunk(i, j, k)
                        if k == KC - 1:
                            last.then_inc(main_done, 1)
                        if before and k == 1:
                            transpose_xa(i, j)
                        if before and k == 3:
                            add_lora(i, j)
                        if before and k == 6:
                            cond_product(i, j)
                else:
                    transpose_xa(i, j)
                    add_lora(i, j)
                    cond_product(i, j)

            pe.wait_ge(ident_ready, 1)
            run_steps(pe, step)


def kernel(x, itok_B_1_198, itok_B_0_6, L0_cond_weights, L1_cond_W, L1_cond_A, L1_cond_Bm, L1_cond_scalings):
    import numpy as np
    import concourse.bacc as bacc
    from concourse.bass_utils import run_bass_kernel_spmd

    nb, c, t = x.shape
    kc = t // P
    nad, r, _ = L1_cond_A.shape
    arrays = {
        "xT": np.ascontiguousarray(np.asarray(x).reshape(nb, c, kc, P).transpose(0, 3, 2, 1)),
        "cond_idx": np.asarray(itok_B_1_198).reshape(1, nb),
        "adapter_idx": np.asarray(itok_B_0_6).reshape(1, nb),
        "cond_w": np.asarray(L0_cond_weights),
        "wT": np.ascontiguousarray(np.asarray(L1_cond_W).reshape(t, kc, P).transpose(2, 1, 0)),
        "lora_a": np.ascontiguousarray(np.asarray(L1_cond_A).reshape(nad, r, kc, P).transpose(3, 0, 2, 1)),
        "lora_b": np.ascontiguousarray(np.asarray(L1_cond_Bm).transpose(0, 2, 1)),
        "scalings": np.asarray(L1_cond_scalings).reshape(1, nad),
    }
    nc = bacc.Bacc("TRN2", target_bir_lowering=False, num_devices=1)
    args = {n: nc.dram_tensor(n, a.shape, mybir.dt.from_np(a.dtype), kind="ExternalInput").ap()
            for n, a in arrays.items()}
    args["out"] = nc.dram_tensor("out", (nb, c, t), mybir.dt.float32, kind="ExternalOutput").ap()
    cond_resid_kernel(nc, **args)
    result = run_bass_kernel_spmd(nc, [arrays], core_ids=[0])
    return result.results[0]["out"]
```

```python
import concourse.bass as bass
from concourse import mybir
from contextlib import ExitStack

P = 128


def cond_resid_kernel(nc, xT, cond_idx, adapter_idx, cond_w, wT, lora_a, lora_b, scalings, out):
    f32 = mybir.dt.float32
    f32r = mybir.dt.float32r
    i32 = mybir.dt.int32
    ALU = mybir.AluOpType
    ACT = mybir.ActivationFunctionType

    NB, _, KC, C = xT.shape
    T = KC * P
    NCOND = cond_w.shape[0]
    NAD, R = lora_a.shape[1], lora_a.shape[3]
    ROW = T + R
    WIDE = T + 2 * R
    FIRST = (ROW + 5) // 6 * 2
    CUTS = [0, FIRST, FIRST + (ROW - FIRST) // 2, ROW]
    NZ = len(CUTS) - 1
    HALF = T // 2
    BANK = 512

    def pieces(par):
        shift = R if par == 0 else 0
        found = []
        for n in range(NZ):
            lo, hi = max(CUTS[n] - shift, 0), min(CUTS[n + 1] - shift, T)
            found.append((lo + shift - CUTS[n], lo, hi))
        return found

    with ExitStack() as ctx:
        def sb(name, shape, dt):
            return ctx.enter_context(nc.sbuf_tensor(name, shape, dt))

        def sem(name):
            return ctx.enter_context(nc.semaphore(name))

        w_raw = sb("w_raw", [P, KC, T], f32)
        w_hi = sb("w_hi", [P, KC, WIDE], f32r)
        w_lo = sb("w_lo", [P, KC, WIDE], f32r)
        a_tab = sb("a_tab", [P, NAD, KC, R], f32)
        a_now = [sb(f"a_now{j}", [P, KC, R], f32) for j in range(2)]
        s_now = [sb(f"s_now{j}", [P, 1], f32) for j in range(2)]
        s_tab = sb("s_tab", [P, NAD], f32)
        cond_sb = sb("cond_sb", [1, NB], i32)
        adapter_sb = sb("adapter_sb", [1, NB], i32)
        ident = sb("ident", [P, P], f32)
        x_raw = [sb(f"x_raw{j}", [P, KC, C], f32) for j in range(2)]
        x_hi = [sb(f"x_hi{j}", [P, KC, C], f32r) for j in range(2)]
        x_lo = [sb(f"x_lo{j}", [P, KC, C], f32r) for j in range(2)]
        c_raw = [sb(f"c_raw{j}", [P, P], f32) for j in range(2)]
        c_hi = [sb(f"c_hi{j}", [P, P], f32r) for j in range(2)]
        c_lo = [sb(f"c_lo{j}", [P, P], f32r) for j in range(2)]
        b_raw = [sb(f"b_raw{j}", [3 * R, T], f32) for j in range(2)]
        b_stack = [sb(f"b_stack{j}", [P, T], f32r) for j in range(2)]
        xa_cols = sb("xa_cols", [P, P], f32)
        xa_stack = sb("xa_stack", [P, P], f32r)
        z_hi = [sb(f"z_hi{j}", [P, T], f32r) for j in range(2)]
        z_lo = [sb(f"z_lo{j}", [P, T], f32r) for j in range(2)]
        o_sb = [sb(f"o_sb{j}", [P, T], f32) for j in range(2)]

        z_ps = [[ctx.enter_context(nc.psum_tensor(f"z_ps{j}_{n}", [P, BANK], f32)) for n in range(NZ)]
                for j in range(2)]
        o_ps = [ctx.enter_context(nc.psum_tensor(f"o_ps{n}", [P, BANK], f32)) for n in range(2)]
        xaT_ps = o_ps[0]

        adapter_landed = sem("adapter_landed")
        cond_landed = sem("cond_landed")
        s_landed = sem("s_landed")
        a_first_landed = [sem(f"a_first_landed{b}") for b in range(2)]
        atab_landed = sem("atab_landed")
        w_landed = [sem(f"w_landed{k}") for k in range(KC)]
        x_landed = [sem(f"x_landed{j}") for j in range(2)]
        c_landed = [sem(f"c_landed{j}") for j in range(2)]
        b_landed = [sem(f"b_landed{j}") for j in range(2)]
        ident_zero = sem("ident_zero")
        ident_ready = sem("ident_ready")
        zeros_ready = sem("zeros_ready")
        w_summed = sem("w_summed")
        w_hi_ready = sem("w_hi_ready")
        w_lo_ready = sem("w_lo_ready")
        x_first_landed = sem("x_first_landed")
        x_first_hi_ready = sem("x_first_hi_ready")
        x_first_lo_ready = sem("x_first_lo_ready")
        x_hi_ready = sem("x_hi_ready")
        x_lo_ready = sem("x_lo_ready")
        a_picked = sem("a_picked")
        s_picked = sem("s_picked")
        a_scaled = sem("a_scaled")
        a_hi_ready = sem("a_hi_ready")
        a_ready = sem("a_ready")
        main_done = sem("main_done")
        xa_hi_ready = sem("xa_hi_ready")
        xa_ready = sem("xa_ready")
        xaT_done = sem("xaT_done")
        xaT_ready = sem("xaT_ready")
        b_hi_ready = sem("b_hi_ready")
        b_ready = sem("b_ready")
        z_done = sem("z_done")
        z_hi_ready = sem("z_hi_ready")
        z_lo_ready = sem("z_lo_ready")
        c_summed = sem("c_summed")
        c_hi_ready = sem("c_hi_ready")
        c_lo_ready = sem("c_lo_ready")
        o_done = sem("o_done")
        o_left = sem("o_left")
        o_right = sem("o_right")
        stored = [sem(f"stored{j}") for j in range(2)]

        block = ctx.enter_context(nc.Block())

        def run_steps(eng, step):
            step(0, 0)
            step(0, 1)
            with eng.Fori(1, NB // 2 - 1) as i:
                step(i, 0)
                step(i, 1)
            step(NB // 2 - 1, 0)
            step(NB // 2 - 1, 1)
            step(NB // 2, 0)

        def exists(i, j, d):
            return not isinstance(i, int) or 0 <= 2 * i + j + d < NB

        def done(i, j, d, per=1):
            return (i * 2 + (j + d + 1)) * per

        def landed(i, j, d, per=1):
            return (i + ((j + d) // 2 + 1)) * (16 * per)

        def final(i, j, d):
            return isinstance(i, int) and 2 * i + j + d == NB - 1

        def bank_order(i, j, d):
            return [2, 1, 0] if final(i, j, d) else [0, 1, 2]

        def half_order(i, j, d):
            return [1, 0] if final(i, j, d) else [0, 1]

        @block.sync
        def _(sp):
            def load_x(i, j, d):
                slot = (j + d) % 2
                b = i * 2 + (j + d)
                if exists(i, j, d - 2):
                    sp.wait_ge(x_lo_ready, done(i, j, d - 2))
                sp.dma_start(x_raw[slot][:, :, :], xT[bass.ds(b, 1), :, :, :].rearrange("b p k c -> (b p) k c"))\
                  .then_inc(x_landed[slot], 16)

            def load_rest(i, j, d):
                slot = (j + d) % 2
                b = i * 2 + (j + d)
                cond = sp.value_load(cond_sb[0:1, bass.ds(b, 1)], min_val=0, max_val=NCOND - 1)
                if exists(i, j, d - 2):
                    sp.wait_ge(c_lo_ready, done(i, j, d - 2))
                sp.dma_start(c_raw[slot][:, :], cond_w[bass.ds(cond, 1), :, :].rearrange("s c d -> (s c) d"))\
                  .then_inc(c_landed[slot], 16)
                adapter = sp.value_load(adapter_sb[0:1, bass.ds(b, 1)], min_val=0, max_val=NAD - 1)
                if exists(i, j, d - 2):
                    sp.wait_ge(b_ready, done(i, j, d - 2))
                for g in range(3):
                    sp.dma_start(b_raw[slot][g * R:(g + 1) * R, :],
                                 lora_b[bass.ds(adapter, 1), :, :].rearrange("a r o -> (a r) o"))\
                      .then_inc(b_landed[slot], 16)

            def step(i, j):
                if exists(i, j, -1) and exists(i, j, 2):
                    load_x(i, j, 2)
                    load_rest(i, j, 2)
                if exists(i, j, -1):
                    slot = (j - 1) % 2
                    b = i * 2 + (j - 1)
                    if final(i, j, -1):
                        for n in half_order(i, j, -1):
                            sp.wait_ge(o_right if n else o_left, NB)
                            sp.dma_start(out[b, :, n * HALF:(n + 1) * HALF], o_sb[slot][:, n * HALF:(n + 1) * HALF])\
                              .then_inc(stored[slot], 16)
                    else:
                        sp.wait_ge(o_left, done(i, j, -1))
                        sp.wait_ge(o_right, done(i, j, -1))
                        sp.dma_start(out[bass.ds(b, 1), :, :].rearrange("b d o -> (b d) o"), o_sb[slot][:, :])\
                          .then_inc(stored[slot], 16)

            sp.dma_start(adapter_sb[:, :], adapter_idx).then_inc(adapter_landed, 16)
            sp.dma_start(x_raw[0][:, 0:KC // 2, :], xT[0, :, 0:KC // 2, :]).then_inc(x_first_landed, 16)
            sp.dma_start(x_raw[0][:, KC // 2:KC, :], xT[0, :, KC // 2:KC, :]).then_inc(x_landed[0], 16)
            sp.dma_start(w_raw[:, 1, :], wT[:, 1, :]).then_inc(w_landed[1], 16)
            sp.wait_ge(adapter_landed, 16)
            for b in range(2):
                adapter = sp.value_load(adapter_sb[0:1, b:b + 1], min_val=0, max_val=NAD - 1)
                sp.dma_start(a_now[b][:, :, :], lora_a[:, bass.ds(adapter, 1), :, :].rearrange("p a k r -> p (a k) r"))\
                  .then_inc(a_first_landed[b], 16)
                sp.dma_start(w_raw[:, 2 + b, :], wT[:, 2 + b, :]).then_inc(w_landed[2 + b], 16)
            sp.dma_start(cond_sb[:, :], cond_idx).then_inc(cond_landed, 16)
            for k in range(4, KC):
                sp.dma_start(w_raw[:, k, :], wT[:, k, :]).then_inc(w_landed[k], 16)
            load_x(0, 0, 1)
            sp.wait_ge(cond_landed, 16)
            load_rest(0, 0, 0)
            load_x(0, 0, 2)
            load_rest(0, 0, 1)
            sp.dma_start(a_tab[:, :, :, :], lora_a).then_inc(atab_landed, 16)
            load_rest(0, 0, 2)
            run_steps(sp, step)
            sp.wait_ge(stored[0], 16 * (NB // 2))
            sp.wait_ge(stored[1], 16 * (NB // 2 + 1))

        @block.gpsimd
        def _(pool):
            def place_a(i, j, d):
                slot = (j + d) % 2
                col = slot * (T + R)
                b = i * 2 + (j + d)
                adapter = pool.value_load(adapter_sb[0:1, bass.ds(b, 1)], min_val=0, max_val=NAD - 1)
                if exists(i, j, d - 2):
                    nc.gpsimd.tensor_copy(a_now[slot][:, :, :],
                                          a_tab[:, bass.ds(adapter, 1), :, :].rearrange("p a k r -> p (a k) r"))\
                        .then_inc(a_picked, 1)
                else:
                    pool.wait_ge(s_landed, 16)
                nc.gpsimd.tensor_copy(s_now[slot][:, :], s_tab[:, bass.ds(adapter, 1)]).then_inc(s_picked, 1)
                if exists(i, j, d - 2):
                    pool.wait_ge(a_picked, done(i, j, d - 2))
                else:
                    pool.wait_ge(a_first_landed[slot], 16)
                pool.wait_ge(s_picked, done(i, j, d))
                nc.gpsimd.tensor_tensor(a_now[slot][:, :, :].rearrange("p k r -> p (k r)"),
                                        a_now[slot][:, :, :].rearrange("p k r -> p (k r)"),
                                        s_now[slot][:, :].to_broadcast([P, KC * R]), ALU.mult).then_inc(a_scaled, 1)
                pool.wait_ge(a_hi_ready, done(i, j, d))
                nc.gpsimd.tensor_tensor(w_lo[:, :, col:col + R], a_now[slot][:, :, :],
                                        w_hi[:, :, col:col + R], ALU.subtract).then_inc(a_ready, 1)

            def add_identity(k):
                pool.wait_ge(w_landed[k], 16)
                nc.gpsimd.tensor_tensor(w_raw[:, k, k * P:(k + 1) * P], w_raw[:, k, k * P:(k + 1) * P],
                                        ident[:, :], ALU.add).then_inc(w_summed, 1)

            def step(i, j):
                if not exists(i, j, -1):
                    place_a(i, j, 1)
                    pool.wait_ge(atab_landed, 16)
                elif exists(i, j, 1):
                    place_a(i, j, 1)

            nc.gpsimd.memset(ident[:, :], 0.0).then_inc(ident_zero, 1)
            pool.wait_ge(ident_zero, 1)
            nc.gpsimd.affine_select(out=ident[:, :], in_=ident[:, :], compare_op=ALU.not_equal, fill=1.0,
                                    base=0, pattern=[[-1, P]], channel_multiplier=1).then_inc(ident_ready, 1)
            nc.gpsimd.memset(xa_cols[:, :], 0.0).then_inc(zeros_ready, 1)
            for slot in range(2):
                nc.gpsimd.memset(b_stack[slot][:, :].bitcast(f32), 0.0).then_inc(zeros_ready, 1)
            pool.wait_ge(ident_ready, 1)
            add_identity(0)
            add_identity(1)
            pool.wait_ge(adapter_landed, 16)
            place_a(0, 0, 0)
            for k in range(2, KC):
                add_identity(k)
            run_steps(pool, step)

        @block.scalar
        def _(act):
            def split_x(i, j, d):
                slot = (j + d) % 2
                act.wait_ge(x_landed[slot], landed(i, j, d))
                if exists(i, j, d - 2):
                    act.wait_ge(main_done, done(i, j, d - 2))
                nc.scalar.activation(x_hi[slot][:, :, :], x_raw[slot][:, :, :], ACT.Copy).then_inc(x_hi_ready, 1)

            def split_a(i, j, d):
                slot = (j + d) % 2
                col = slot * (T + R)
                act.wait_ge(a_scaled, done(i, j, d))
                if exists(i, j, d - 2):
                    act.wait_ge(main_done, done(i, j, d - 2))
                nc.scalar.activation(w_hi[:, :, col:col + R], a_now[slot][:, :, :], ACT.Copy)\
                    .then_inc(a_hi_ready, 1)

            def step(i, j):
                if exists(i, j, 1):
                    split_x(i, j, 1)
                    split_a(i, j, 1)
                if exists(i, j, 0):
                    slot = j % 2
                    act.wait_ge(b_landed[slot], landed(i, j, 0, 3))
                    if exists(i, j, -2):
                        act.wait_ge(z_done, done(i, j, -2, NZ))
                    else:
                        act.wait_ge(zeros_ready, 3)
                    nc.scalar.activation(b_stack[slot][0:3 * R, :], b_raw[slot][:, :], ACT.Copy)\
                        .then_inc(b_hi_ready, 1)
                    act.wait_ge(c_summed, done(i, j, 0))
                    if exists(i, j, -2):
                        act.wait_ge(o_done, done(i, j, -2, 2))
                    nc.scalar.activation(c_hi[slot][:, :], c_raw[slot][:, :], ACT.Copy).then_inc(c_hi_ready, 1)
                if exists(i, j, -1):
                    slot = (j - 1) % 2
                    act.wait_ge(xaT_done, done(i, j, -1))
                    nc.scalar.activation(xa_stack[:, :], xaT_ps[:, 0:P], ACT.Copy).then_inc(xaT_ready, 1)
                    for m, n in enumerate(bank_order(i, j, -1)):
                        at, lo, hi = pieces(slot)[n]
                        act.wait_ge(z_done, done(i, j, -2, NZ) + (m + 1))
                        nc.scalar.activation(z_hi[slot][:, lo:hi], z_ps[slot][n][:, at:at + hi - lo], ACT.Copy)\
                            .then_inc(z_hi_ready, 1)
                    act.wait_ge(o_done, done(i, j, -2, 2) + (half_order(i, j, -1).index(0) + 1))
                    if exists(i, j, -3):
                        act.wait_ge(stored[slot], landed(i, j, -3))
                    nc.scalar.activation(o_sb[slot][:, 0:HALF], o_ps[0][:, :], ACT.Copy).then_inc(o_left, 1)

            act.dma_start(w_raw[:, 0, :], wT[:, 0, :]).then_inc(w_landed[0], 16)
            act.dma_start(s_tab[:, :], scalings.to_broadcast([P, NAD])).then_inc(s_landed, 16)
            act.wait_ge(x_first_landed, 16)
            nc.scalar.activation(x_hi[0][:, 0:KC // 2, :], x_raw[0][:, 0:KC // 2, :], ACT.Copy)\
                .then_inc(x_first_hi_ready, 1)
            for k in range(KC):
                act.wait_ge(w_summed, k + 1)
                nc.scalar.activation(w_hi[:, k, R:R + T], w_raw[:, k, :], ACT.Copy).then_inc(w_hi_ready, 1)
                if k == 0:
                    act.wait_ge(x_landed[0], 16)
                    nc.scalar.activation(x_hi[0][:, KC // 2:KC, :], x_raw[0][:, KC // 2:KC, :], ACT.Copy)\
                        .then_inc(x_hi_ready, 1)
                    split_a(0, 0, 0)
            run_steps(act, step)

        @block.vector
        def _(dve):
            def split_x(i, j, d):
                slot = (j + d) % 2
                dve.wait_ge(x_hi_ready, done(i, j, d))
                nc.vector.tensor_tensor(x_lo[slot][:, :, :], x_raw[slot][:, :, :], x_hi[slot][:, :, :],
                                        ALU.subtract).then_inc(x_lo_ready, 1)

            def step(i, j):
                if exists(i, j, -1):
                    slot = (j - 1) % 2
                    n, at = (0, 0) if slot == 0 else (NZ - 1, ROW - R - CUTS[NZ - 1])
                    xa = z_ps[slot][n][:, at:at + R]
                    dve.wait_ge(main_done, done(i, j, -1))
                    if exists(i, j, -2):
                        dve.wait_ge(xaT_done, done(i, j, -2))
                    else:
                        dve.wait_ge(zeros_ready, 3)
                    nc.vector.tensor_copy(xa_cols[:, 0:R].bitcast(f32r), xa)
                    nc.vector.tensor_copy(xa_cols[:, 2 * R:3 * R].bitcast(f32r), xa).then_inc(xa_hi_ready, 1)
                    dve.wait_ge(xa_hi_ready, done(i, j, -1))
                    nc.vector.tensor_tensor(xa_cols[:, R:2 * R].bitcast(f32r), xa, xa_cols[:, 0:R],
                                            ALU.subtract).then_inc(xa_ready, 1)
                if exists(i, j, 0):
                    slot = j % 2
                    dve.wait_ge(c_landed[slot], landed(i, j, 0))
                    nc.vector.tensor_tensor(c_raw[slot][:, :], c_raw[slot][:, :], ident[:, :], ALU.add)\
                        .then_inc(c_summed, 1)
                if exists(i, j, 1):
                    split_x(i, j, 1)
                if exists(i, j, 0):
                    dve.wait_ge(b_hi_ready, done(i, j, 0))
                    nc.vector.tensor_tensor(b_stack[slot][2 * R:3 * R, :], b_raw[slot][2 * R:3 * R, :],
                                            b_stack[slot][2 * R:3 * R, :], ALU.subtract).then_inc(b_ready, 1)
                    dve.wait_ge(c_hi_ready, done(i, j, 0))
                    nc.vector.tensor_tensor(c_lo[slot][:, :], c_raw[slot][:, :], c_hi[slot][:, :], ALU.subtract)\
                        .then_inc(c_lo_ready, 1)
                if exists(i, j, -1):
                    slot = (j - 1) % 2
                    for m, n in enumerate(bank_order(i, j, -1)):
                        if final(i, j, -1) and m == NZ - 1:
                            evacuate_right(i, j, slot)
                        at, lo, hi = pieces(slot)[n]
                        dve.wait_ge(z_hi_ready, done(i, j, -2, NZ) + (m + 1))
                        nc.vector.tensor_tensor(z_lo[slot][:, lo:hi], z_ps[slot][n][:, at:at + hi - lo],
                                                z_hi[slot][:, lo:hi], ALU.subtract).then_inc(z_lo_ready, 1)
                    if not final(i, j, -1):
                        evacuate_right(i, j, slot)

            def evacuate_right(i, j, slot):
                dve.wait_ge(o_done, done(i, j, -2, 2) + (half_order(i, j, -1).index(1) + 1))
                if exists(i, j, -3):
                    dve.wait_ge(stored[slot], landed(i, j, -3))
                nc.vector.tensor_copy(o_sb[slot][:, HALF:T], o_ps[1][:, :]).then_inc(o_right, 1)

            dve.wait_ge(x_first_hi_ready, 1)
            nc.vector.tensor_tensor(x_lo[0][:, 0:KC // 2, :], x_raw[0][:, 0:KC // 2, :],
                                    x_hi[0][:, 0:KC // 2, :], ALU.subtract).then_inc(x_first_lo_ready, 1)
            for k in range(KC):
                dve.wait_ge(w_hi_ready, k + 1)
                nc.vector.tensor_tensor(w_lo[:, k, R:R + T], w_raw[:, k, :], w_hi[:, k, R:R + T],
                                        ALU.subtract).then_inc(w_lo_ready, 1)
                if k == 0:
                    dve.wait_ge(x_hi_ready, 1)
                    nc.vector.tensor_tensor(x_lo[0][:, KC // 2:KC, :], x_raw[0][:, KC // 2:KC, :],
                                            x_hi[0][:, KC // 2:KC, :], ALU.subtract).then_inc(x_lo_ready, 1)
            dve.wait_ge(ident_ready, 1)
            run_steps(dve, step)

        @block.tensor
        def _(pe):
            def main_product(i, j, k, order, by_bank):
                slot = j % 2
                first = 0 if slot == 0 else R
                parts = ((x_hi, w_hi), (x_hi, w_lo), (x_lo, w_hi))
                if by_bank:
                    todo = [(n, left, right) for n in order for left, right in parts]
                else:
                    todo = [(n, left, right) for left, right in parts for n in order]
                for n, left, right in todo:
                    last = nc.tensor.matmul(z_ps[slot][n][:, 0:CUTS[n + 1] - CUTS[n]], left[slot][:, k, :],
                                            right[:, k, first + CUTS[n]:first + CUTS[n + 1]],
                                            start=(k == 0 and left is x_hi and right is w_hi),
                                            stop=(k == KC - 1 and left is x_lo))
                return last

            def transpose_xa(i, j, d):
                pe.wait_ge(xa_ready, done(i, j, d))
                if exists(i, j, d - 1):
                    pe.wait_ge(o_left, done(i, j, d - 1))
                nc.tensor.transpose(xaT_ps[:, 0:P], xa_cols[:, :], ident[:, :]).then_inc(xaT_done, 1)

            def add_lora(i, j, d, banks):
                slot = (j + d) % 2
                pe.wait_ge(xaT_ready, done(i, j, d))
                pe.wait_ge(b_ready, done(i, j, d))
                for n in banks:
                    at, lo, hi = pieces(slot)[n]
                    nc.tensor.matmul(z_ps[slot][n][:, at:at + hi - lo], xa_stack[:, :], b_stack[slot][:, lo:hi],
                                     start=False, stop=True, skip_group_check=True).then_inc(z_done, 1)

            def cond_product(i, j, d, halves):
                slot = (j + d) % 2
                pe.wait_ge(c_lo_ready, done(i, j, d))
                for n in halves:
                    if exists(i, j, d - 1):
                        pe.wait_ge(o_right if n else o_left, done(i, j, d - 1))
                    cols = slice(n * HALF, (n + 1) * HALF)
                    order = bank_order(i, j, d)
                    need = 1 + max(order.index(m) for m, (_, lo, hi) in enumerate(pieces(slot))
                                   if lo < cols.stop and hi > cols.start)
                    pe.wait_ge(z_lo_ready, done(i, j, d - 1, NZ) + need)
                    nc.tensor.matmul(o_ps[n][:, :], c_hi[slot][:, :], z_hi[slot][:, cols], start=True, stop=False)
                    nc.tensor.matmul(o_ps[n][:, :], c_hi[slot][:, :], z_lo[slot][:, cols], start=False, stop=False)
                    nc.tensor.matmul(o_ps[n][:, :], c_lo[slot][:, :], z_hi[slot][:, cols], start=False, stop=True)\
                        .then_inc(o_done, 1)

            def main_waits(i, j):
                pe.wait_ge(x_lo_ready, done(i, j, 0))
                if exists(i, j, -2):
                    pe.wait_ge(z_lo_ready, done(i, j, -2, NZ))

            def step(i, j):
                if not exists(i, j, -1):
                    pe.wait_ge(x_first_lo_ready, 1)
                    for k in range(KC):
                        pe.wait_ge(w_lo_ready, k + 1)
                        if k == KC // 2:
                            pe.wait_ge(x_lo_ready, 1)
                        if k == 0:
                            main_product(i, j, k, [1, 2], True)
                            pe.wait_ge(a_ready, 1)
                            main_product(i, j, k, [0], True)
                        else:
                            last = main_product(i, j, k, [0, 1, 2], False)
                    last.then_inc(main_done, 1)
                elif final(i, j, 0):
                    main_waits(i, j)
                    pe.wait_ge(a_ready, done(i, j, 0))
                    after = {(0, 2): lambda: transpose_xa(i, j, -1), (0, 4): lambda: add_lora(i, j, -1, [0, 1, 2]),
                             (1, 4): lambda: cond_product(i, j, -1, [0, 1]), (1, 7): lambda: transpose_xa(i, j, 0),
                             (2, 1): lambda: add_lora(i, j, 0, [2, 1]), (2, 6): lambda: cond_product(i, j, 0, [1])}
                    for m, n in enumerate(bank_order(i, j, 0)):
                        for k in range(KC):
                            last = main_product(i, j, k, [n], True)
                            if m == 0 and k == KC - 1:
                                last.then_inc(main_done, 1)
                            if (m, k) in after:
                                after[m, k]()
                elif exists(i, j, 0):
                    main_waits(i, j)
                    pe.wait_ge(a_ready, done(i, j, 0))
                    for k in range(KC):
                        last = main_product(i, j, k, [0, 1, 2], False)
                        if k == KC - 1:
                            last.then_inc(main_done, 1)
                        if k == 1:
                            transpose_xa(i, j, -1)
                        if k == 3:
                            add_lora(i, j, -1, [0, 1, 2])
                        if k == 6:
                            cond_product(i, j, -1, [0, 1])
                else:
                    add_lora(i, j, -1, [0])
                    cond_product(i, j, -1, [0])

            pe.wait_ge(ident_ready, 1)
            run_steps(pe, step)


def kernel(x, itok_B_1_198, itok_B_0_6, L0_cond_weights, L1_cond_W, L1_cond_A, L1_cond_Bm, L1_cond_scalings):
    import numpy as np
    import concourse.bacc as bacc
    from concourse.bass_utils import run_bass_kernel_spmd

    nb, c, t = x.shape
    kc = t // P
    nad, r, _ = L1_cond_A.shape
    arrays = {
        "xT": np.ascontiguousarray(np.asarray(x).reshape(nb, c, kc, P).transpose(0, 3, 2, 1)),
        "cond_idx": np.asarray(itok_B_1_198).reshape(1, nb),
        "adapter_idx": np.asarray(itok_B_0_6).reshape(1, nb),
        "cond_w": np.asarray(L0_cond_weights),
        "wT": np.ascontiguousarray(np.asarray(L1_cond_W).reshape(t, kc, P).transpose(2, 1, 0)),
        "lora_a": np.ascontiguousarray(np.asarray(L1_cond_A).reshape(nad, r, kc, P).transpose(3, 0, 2, 1)),
        "lora_b": np.ascontiguousarray(np.asarray(L1_cond_Bm).transpose(0, 2, 1)),
        "scalings": np.asarray(L1_cond_scalings).reshape(1, nad),
    }
    nc = bacc.Bacc("TRN2", target_bir_lowering=False, num_devices=1)
    args = {n: nc.dram_tensor(n, a.shape, mybir.dt.from_np(a.dtype), kind="ExternalInput").ap()
            for n, a in arrays.items()}
    args["out"] = nc.dram_tensor("out", (nb, c, t), mybir.dt.float32, kind="ExternalOutput").ap()
    cond_resid_kernel(nc, **args)
    result = run_bass_kernel_spmd(nc, [arrays], core_ids=[0])
    return result.results[0]["out"]
```
